# Optimizing a Trainium2 kernel written in Bass

```python
import numpy as np
import jax
import jax.numpy as jnp

def _softmax(x, axis=-1):
    return jax.nn.softmax(x, axis=axis)

def _gelu(x):
    return jax.nn.gelu(x, approximate=True)

def _silu(x):
    return jax.nn.silu(x)

def _sigmoid(x):
    return jax.nn.sigmoid(x)

def _layernorm(x, axis=-1, eps=1e-05):
    m = jnp.mean(x, axis=axis, keepdims=True)
    v = jnp.var(x, axis=axis, keepdims=True)
    return (x - m) / jnp.sqrt(v + eps)

def _scatter_add(tgt, idx, src, axis=0):
    return tgt.at[idx].add(src)

def _segment_sum(src, seg, n):
    return jax.ops.segment_sum(src, seg, n)
kernel_name = 'mk_prb_d1_jaxref_r8_9fe5c6'

def setup_inputs(seed: int=0):
    np.random.seed(seed)
    _w = jnp.asarray

    def _L0_attn_setup():
        import jax, jax.numpy as jnp
        import numpy as np
        D_MODEL = 128
        N_HEADS = 16
        D_HEAD = D_MODEL // N_HEADS
        BATCH = 2
        SEQ = 256

        def _evolved_attention(x, Wq, bq, Wk, bk, Wv, bv, Wo, bo, Wt, bt, Wg, bg):
            B, S, D = x.shape
            H, dh = (N_HEADS, D_HEAD)

            def heads(y):
                return y.reshape(B, S, H, dh).transpose(0, 2, 1, 3)
            q = heads(x @ Wq + bq)
            k = heads(x @ Wk + bk)
            v = heads(x @ Wv + bv)
            qn = q / jnp.maximum(jnp.linalg.norm(q, axis=-1, keepdims=True), 1e-12)
            kn = k / jnp.maximum(jnp.linalg.norm(k, axis=-1, keepdims=True), 1e-12)
            scores = jnp.einsum('bhqd,bhkd->bhqk', qn, kn)
            temp = jax.nn.sigmoid(x.mean(axis=1) @ Wt + bt) + 0.5
            scores = scores / temp[:, None, None, :]
            kk = max(1, S // 4)
            vals, idx = jax.lax.top_k(scores, kk)
            w = jax.nn.softmax(vals, axis=-1)
            rows = jnp.arange(B * H * S)[:, None]
            attn = jnp.zeros((B * H * S, S), scores.dtype).at[rows, idx.reshape(-1, kk)].set(w.reshape(-1, kk)).reshape(B, H, S, S)
            out = jnp.einsum('bhqk,bhkd->bhqd', attn, v)
            out = out.transpose(0, 2, 1, 3).reshape(B, S, D)
            out = out @ Wo + bo
            gate = jax.nn.sigmoid(x @ Wg + bg)
            return gate * out + (1.0 - gate) * x
        key = jax.random.key(seed)
        ks = jax.random.split(key, 16)
        s = 0.02
        d = D_MODEL
        return {'x': jax.random.normal(ks[0], (BATCH, SEQ, d), jnp.float32), 'Wq': jax.random.normal(ks[1], (d, d), jnp.float32) * s, 'bq': jnp.zeros((d,), jnp.float32), 'Wk': jax.random.normal(ks[2], (d, d), jnp.float32) * s, 'bk': jnp.zeros((d,), jnp.float32), 'Wv': jax.random.normal(ks[3], (d, d), jnp.float32) * s, 'bv': jnp.zeros((d,), jnp.float32), 'Wo': jax.random.normal(ks[4], (d, d), jnp.float32) * s, 'bo': jnp.zeros((d,), jnp.float32), 'Wt': jax.random.normal(ks[5], (d, 1), jnp.float32) * s, 'bt': jnp.zeros((1,), jnp.float32), 'Wg': jax.random.normal(ks[6], (d, d), jnp.float32) * s, 'bg': jnp.zeros((d,), jnp.float32)}
    _L0_attn_in = _L0_attn_setup()

    def _L0_ffn_setup():
        import jax, jax.numpy as jnp
        import numpy as np
        key = jax.random.key(seed)
        kx, kw = jax.random.split(key)
        x = jax.random.normal(kx, (32, 512, 128), dtype=jnp.float32)
        weight = jax.random.normal(kw, (128, 128), dtype=jnp.float32) * 0.01
        return {'x': x, 'weight': weight}
    _L0_ffn_in = _L0_ffn_setup()
    _d = {'L0_attn_x': _L0_attn_in['x'], 'L0_attn_Wq': _L0_attn_in['Wq'], 'L0_attn_bq': _L0_attn_in['bq'], 'L0_attn_Wk': _L0_attn_in['Wk'], 'L0_attn_bk': _L0_attn_in['bk'], 'L0_attn_Wv': _L0_attn_in['Wv'], 'L0_attn_bv': _L0_attn_in['bv'], 'L0_attn_Wo': _L0_attn_in['Wo'], 'L0_attn_bo': _L0_attn_in['bo'], 'L0_attn_Wt': _L0_attn_in['Wt'], 'L0_attn_bt': _L0_attn_in['bt'], 'L0_attn_Wg': _L0_attn_in['Wg'], 'L0_attn_bg': _L0_attn_in['bg'], 'L0_ffn_weight': _L0_ffn_in['weight']}
    _x0 = _d['L0_attn_x']
    _d['L0_attn_x'] = jax.random.normal(jax.random.fold_in(jax.random.key(seed), 1), (32, 256, 128), dtype=_x0.dtype)
    del _x0
    return _d

def reference(L0_attn_x, L0_attn_Wq, L0_attn_bq, L0_attn_Wk, L0_attn_bk, L0_attn_Wv, L0_attn_bv, L0_attn_Wo, L0_attn_bo, L0_attn_Wt, L0_attn_bt, L0_attn_Wg, L0_attn_bg, L0_ffn_weight):

    def _L0_attn_ref(x, Wq, bq, Wk, bk, Wv, bv, Wo, bo, Wt, bt, Wg, bg):
        import jax, jax.numpy as jnp
        import numpy as np
        D_MODEL = 128
        N_HEADS = 16
        D_HEAD = D_MODEL // N_HEADS
        BATCH = 2
        SEQ = 256

        def _evolved_attention(x, Wq, bq, Wk, bk, Wv, bv, Wo, bo, Wt, bt, Wg, bg):
            B, S, D = x.shape
            H, dh = (N_HEADS, D_HEAD)

            def heads(y):
                return y.reshape(B, S, H, dh).transpose(0, 2, 1, 3)
            q = heads(x @ Wq + bq)
            k = heads(x @ Wk + bk)
            v = heads(x @ Wv + bv)
            qn = q / jnp.maximum(jnp.linalg.norm(q, axis=-1, keepdims=True), 1e-12)
            kn = k / jnp.maximum(jnp.linalg.norm(k, axis=-1, keepdims=True), 1e-12)
            scores = jnp.einsum('bhqd,bhkd->bhqk', qn, kn)
            temp = jax.nn.sigmoid(x.mean(axis=1) @ Wt + bt) + 0.5
            scores = scores / temp[:, None, None, :]
            kk = max(1, S // 4)
            vals, idx = jax.lax.top_k(scores, kk)
            w = jax.nn.softmax(vals, axis=-1)
            rows = jnp.arange(B * H * S)[:, None]
            attn = jnp.zeros((B * H * S, S), scores.dtype).at[rows, idx.reshape(-1, kk)].set(w.reshape(-1, kk)).reshape(B, H, S, S)
            out = jnp.einsum('bhqk,bhkd->bhqd', attn, v)
            out = out.transpose(0, 2, 1, 3).reshape(B, S, D)
            out = out @ Wo + bo
            gate = jax.nn.sigmoid(x @ Wg + bg)
            return gate * out + (1.0 - gate) * x
        return _evolved_attention(x, Wq, bq, Wk, bk, Wv, bv, Wo, bo, Wt, bt, Wg, bg)

    def _L0_ffn_ref(x, weight):
        import jax, jax.numpy as jnp
        import numpy as np
        b_weight = jnp.sign(weight)
        return jnp.einsum('bsi,oi->bso', x, b_weight)
    x = L0_attn_x
    xn = _layernorm(x, axis=-1)
    x = x + _L0_attn_ref(xn, L0_attn_Wq, L0_attn_bq, L0_attn_Wk, L0_attn_bk, L0_attn_Wv, L0_attn_bv, L0_attn_Wo, L0_attn_bo, L0_attn_Wt, L0_attn_bt, L0_attn_Wg, L0_attn_bg) + _L0_ffn_ref(xn, L0_ffn_weight)
    return x

_drawn_inputs = setup_inputs


def setup_inputs(seed=0):
    import zlib

    import numpy as np

    out = dict(_drawn_inputs(seed))
    spreads = {'L0_attn_bq': (0.0, 2.0),
     'L0_attn_bk': (0.0, 2.0),
     'L0_attn_bv': (0.0, 0.8),
     'L0_attn_bo': (0.0, 0.8),
     'L0_attn_bg': (0.0, 2.0)}
    factors = {'L0_attn_Wq': 23.027,
     'L0_attn_Wk': 8.0,
     'L0_attn_Wv': 8.0,
     'L0_attn_Wo': 8.0,
     'L0_attn_Wt': 200.0,
     'L0_attn_Wg': 8.0}
    for name, (base, spread) in spreads.items():
        noise = np.random.default_rng([zlib.crc32(name.encode()), seed]).standard_normal(out[name].shape)
        drawn = base * np.exp(spread * noise) if base else spread * noise
        out[name] = jnp.asarray(drawn.astype(out[name].dtype))
    for name, factor in factors.items():
        out[name] = (out[name] * factor).astype(out[name].dtype)
    return out
```

```python
from contextlib import ExitStack

import concourse.bass as bass
from concourse import mybir

P = 128
F32 = mybir.dt.float32
BF16 = mybir.dt.bfloat16
ALU = mybir.AluOpType
ACT = mybir.ActivationFunctionType
AX = mybir.AxisListType

B, S, D = 32, 256, 128
H, DH = 16, 8
KEEP = S // 4
T = S // P
PARTS = 3
STACK = PARTS * PARTS * DH
EPS_LN = 1e-5
NORM_FLOOR = 1e-12
Q_SCALE = 0.25
REMOVED = -4.0
IS_REMOVED = -2.0
N_DMA_STACK = 2 * PARTS * PARTS
CREDIT = 1
DMA_CREDIT = 16


def build(nc, x, Wq, bq, Wk, bk, Wv, bv, Wo, bo, Wt, bt, Wg, bg, Wf, out):
    ctx = ExitStack()
    with ctx:
        def sb(name, shape, dt=F32):
            return ctx.enter_context(nc.sbuf_tensor(name, shape, dt))

        def psum(name):
            return ctx.enter_context(nc.psum_tensor(name, [P, 512], F32))

        def sem(name):
            return ctx.enter_context(nc.semaphore(name))

        ident = sb("ident", [P, P])
        w_all = sb("w_all", [P, 4 * D])
        w_ffn_raw = sb("w_ffn_raw", [P, D])
        w_ffn_sign = sb("w_ffn_sign", [P, D])
        w_ffn = sb("w_ffn", [P, D])
        w_o = sb("w_o", [P, D])
        wt_col = sb("wt_col", [P, 1])
        wt_wide = sb("wt_wide", [P, P])
        bias_all = sb("bias_all", [P, 4 * D])
        bias_o = sb("bias_o", [P, T, D])
        bias_t = sb("bias_t", [P, 1])
        ones_col = sb("ones_col", [P, 1])
        neg_half = sb("neg_half", [P, 4 * H])
        x_in = sb("x_in", [P, T, D])
        bn = sb("bn", [P, T, 6])
        mv = sb("mv", [P, T, 2])
        var_eps = sb("var_eps", [P, T])
        rstd0 = sb("rstd0", [P, T])
        rstd_t = sb("rstd_t", [P, T])
        rstd = sb("rstd", [P, T])
        xn = sb("xn", [P, T, D])
        xnT = sb("xnT", [P, S])
        xsum = sb("xsum", [P, 1])
        qkvg = sb("qkvg", [P, T, 4 * D])
        v_ext = sb("v_ext", [P, T, H, DH + 1])
        sq = sb("sq", [P, T, 2 * D])
        norm2 = sb("norm2", [P, T * 2 * H])
        inv0 = sb("inv0", [P, T * 2 * H])
        inv_t = sb("inv_t", [P, T * 2 * H])
        inv = sb("inv", [P, T * 2 * H])
        qkn = sb("qkn", [P, T, 2 * D])
        rest = sb("rest", [P, 2 * S])
        parts = sb("parts", [P, PARTS, 2 * S], BF16)
        q_stack = sb("q_stack", [STACK, H * S], BF16)
        k_stack = sb("k_stack", [STACK, H * S], BF16)
        gate_e = sb("gate_e", [P, T, D])
        gate = sb("gate", [P, T, D])
        temp_w = sb("temp_w", [P, 6])
        exp_scale = sb("exp_scale", [P, 1])
        work = sb("work", [P, T, S])
        top8 = sb("top8", [P, T, 8])
        expd = sb("expd", [P, T, S])
        probs = sb("probs", [P, T, S])
        probsT = sb("probsT", [P, T, S])
        copied_mark = sb("copied_mark", [P, 1])
        rden = sb("rden", [P, T])
        attn = sb("attn", [P, T, D])
        attnT = sb("attnT", [P, S])
        mix = sb("mix", [P, T, D])
        base = sb("base", [P, T, D])
        res = sb("res", [P, T, D])

        p_tr = psum("p_tr")
        p_proj = [psum(f"p_proj{t}") for t in range(T)]
        p_score = [psum(f"p_score{t}") for t in range(T)]
        p_prT = [psum(f"p_prT{t}") for t in range(T)]
        p_small = psum("p_small")

        s_const = sem("s_const")
        s_ident0 = sem("s_ident0")
        s_ident = sem("s_ident")
        s_setup = sem("s_setup")
        s_wfT = sem("s_wfT")
        s_wsign = sem("s_wsign")
        s_x = sem("s_x")
        s_var = sem("s_var")
        s_rstd0 = sem("s_rstd0")
        s_xn = sem("s_xn")
        s_xT = sem("s_xT")
        s_xnT = sem("s_xnT")
        s_xsum = sem("s_xsum")
        s_proj = sem("s_proj")
        s_z = sem("s_z")
        s_qkvg = sem("s_qkvg")
        s_vext = sem("s_vext")
        s_sq = sem("s_sq")
        s_norm2 = sem("s_norm2")
        s_inv0 = sem("s_inv0")
        s_qkn = sem("s_qkn")
        s_qkT = sem("s_qkT")
        s_rest = sem("s_rest")
        s_parts = sem("s_parts")
        s_pchain = sem("s_pchain")
        s_stack = sem("s_stack")
        s_gexp = sem("s_gexp")
        s_tz = sem("s_tz")
        s_texp = sem("s_texp")
        s_escale = sem("s_escale")
        s_fchain = sem("s_fchain")
        s_score = sem("s_score")
        s_copied = sem("s_copied")
        s_round = [sem(f"s_round{t}") for t in range(T)]
        s_exp = sem("s_exp")
        s_hchain = sem("s_hchain")
        s_probs = sem("s_probs")
        s_prT = sem("s_prT")
        s_prTc = sem("s_prTc")
        s_av = sem("s_av")
        s_attn = sem("s_attn")
        s_aT = sem("s_aT")
        s_aTc = sem("s_aTc")
        s_y = sem("s_y")
        s_bchain = sem("s_bchain")
        s_res = sem("s_res")
        s_out = sem("s_out")

        x_v = x.rearrange("b (t p) d -> b p t d", p=P)
        out_v = out.rearrange("b (t p) d -> b p t d", p=P)
        N_CONST = 14

        def chain(eng, semaphore):
            eng.sem_clear(semaphore)
            count = [0]

            def link(ins):
                count[0] += 1
                ins.then_inc(semaphore, 1)
                eng.wait_ge(semaphore, count[0])
            return link

        block = ctx.enter_context(nc.Block())

        @block.sync
        def _(sp):
            for handed_back in (s_out, s_stack):
                sp.sem_inc(handed_back, DMA_CREDIT)
            for i, w in enumerate((Wq, Wk, Wv, Wg)):
                sp.dma_start(w_all[:, i * D:(i + 1) * D], w).then_inc(s_const, 16)
            for i, v in enumerate((bq, bk, bv, bg)):
                sp.dma_start(bias_all[:, i * D:(i + 1) * D],
                             v.rearrange("(a d) -> a d", a=1).broadcast_to([P, D])).then_inc(s_const, 16)
            for t in range(T):
                sp.dma_start(bias_o[:, t, :], bo.rearrange("(a d) -> a d", a=1).broadcast_to([P, D])).then_inc(s_const, 16)
            sp.dma_start(bias_t[:, :], bt.rearrange("(a d) -> a d", a=1).broadcast_to([P, 1])).then_inc(s_const, 16)
            sp.dma_start(w_o[:, :], Wo).then_inc(s_const, 16)
            sp.dma_start(w_ffn_raw[:, :], Wf).then_inc(s_const, 16)
            sp.dma_start(wt_col[:, :], Wt).then_inc(s_const, 16)
            with sp.Fori(0, B) as b:
                sp.wait_ge(s_res, b + CREDIT)
                sp.dma_start(x_in[:, :, :], x_v[b]).then_inc(s_x, 16)
                sp.wait_ge(s_parts, b + 1)
                for i in range(PARTS):
                    for j in range(PARTS):
                        r0 = (i * PARTS + j) * DH
                        for dst, part, c0 in ((q_stack, i, 0), (k_stack, j, S)):
                            sp.dma_start(dst[r0:r0 + DH, :].rearrange("d (h s) -> d h s", h=H),
                                         parts[:, part, c0:c0 + S]).then_inc(s_stack, 16)
                sp.wait_ge(s_res, b + 1 + CREDIT)
                sp.dma_start(out_v[b], res[:, :, :]).then_inc(s_out, 16)
            sp.wait_ge(s_out, 16 * B + DMA_CREDIT)

        @block.gpsimd
        def _(pool):
            pool.memset(ident[:, :], 0.0).then_inc(s_ident0, 1)
            pool.wait_ge(s_ident0, 1)
            pool.affine_select(out=ident[:, :], in_=ident[:, :], compare_op=ALU.not_equal, fill=1.0, base=0,
                               pattern=[[-1, P]], channel_multiplier=1).then_inc(s_ident, 1)
            pool.memset(neg_half[:, :], -0.5).then_inc(s_ident, 1)
            pool.memset(ones_col[:, :], 1.0).then_inc(s_ident, 1)
            pool.memset(v_ext[:, :, :, DH:DH + 1], 1.0).then_inc(s_ident, 1)
            pool.wait_ge(s_ident, 4)
            with pool.Fori(0, B) as n:
                link = chain(pool, s_pchain)
                pool.wait_ge(s_var, n + 1)
                pool.tensor_tensor(rstd0[:, :], var_eps[:, :], neg_half[:, 0:T], ALU.pow).then_inc(s_rstd0, 1)
                pool.wait_ge(s_qkvg, 2 * n + 2)
                pool.tensor_tensor(sq[:, :, :], qkvg[:, :, 0:2 * D], qkvg[:, :, 0:2 * D], ALU.mult).then_inc(s_sq, 1)
                pool.wait_ge(s_norm2, n + 1)
                pool.tensor_tensor(inv0[:, :], norm2[:, :], neg_half[:, :], ALU.pow).then_inc(s_inv0, 1)
                pool.wait_ge(s_rest, 2 * n + 2)
                pool.wait_ge(s_stack, 16 * N_DMA_STACK * n + DMA_CREDIT)
                for i in range(PARTS - 1):
                    link(pool.tensor_tensor(parts[:, i, :], rest[:, :], ones_col[:, 0:1].broadcast_to([P, 2 * S]), ALU.mult))
                    link(pool.tensor_tensor(rest[:, :], rest[:, :], parts[:, i, :], ALU.subtract))
                pool.tensor_copy(parts[:, PARTS - 1, :], rest[:, :]).then_inc(s_parts, 1)

        @block.tensor
        def _(pe):
            pe.sem_inc(s_prT, CREDIT)
            pe.wait_ge(s_const, 16 * N_CONST)
            pe.wait_ge(s_ident, 4)
            pe.transpose(p_tr[:, 0:P], w_ffn_raw[:, :], ident[:, :]).then_inc(s_wfT, 1)
            pe.wait_ge(s_setup, 2)
            with pe.Fori(0, B) as n:
                pe.wait_ge(s_xn, n + 1)
                for t in range(T):
                    mm = pe.transpose(p_tr[:, t * P:(t + 1) * P], xn[:, t, :], ident[:, :])
                mm.then_inc(s_xT, 1)
                pe.wait_ge(s_xnT, n + 1)
                for t in range(T):
                    pe.matmul(p_proj[t][:, :], xnT[:, t * P:(t + 1) * P], w_all[:, :], start=True, stop=True).then_inc(s_proj, 1)
                pe.wait_ge(s_xsum, n + 1)
                pe.matmul(p_small[:, 32:33], wt_wide[:, :], xsum[:, :], start=True, stop=True).then_inc(s_z, 1)
                pe.wait_ge(s_qkn, 2 * n + 2)
                for c in range(2):
                    for t in range(T):
                        mm = pe.transpose(p_tr[:, (c * T + t) * P:(c * T + t + 1) * P], qkn[:, t, c * D:(c + 1) * D], ident[:, :])
                mm.then_inc(s_qkT, 1)
                with pe.Fori(0, H) as h:
                    g = n * H + h
                    pe.wait_ge(s_stack, 16 * N_DMA_STACK * (n + 1) + DMA_CREDIT)
                    for t in range(T):
                        pe.wait_ge(s_probs, 2 * g + CREDIT)
                        pe.wait_ge(s_exp, 2 * g + CREDIT)
                        pe.matmul(p_score[t][:, 0:S], q_stack[:, bass.ds(h * S + t * P, P)], k_stack[:, bass.ds(h * S, S)],
                                  start=True, stop=True).then_inc(s_score, 1)
                    for t in range(T):
                        pe.wait_ge(s_probs, 2 * g + t + 1 + CREDIT)
                        for j in range(T):
                            mm = pe.transpose(p_prT[t][:, j * P:(j + 1) * P], probs[:, t, j * P:(j + 1) * P], ident[:, :])
                        mm.then_inc(s_prT, 1)
                    for t in range(T):
                        pe.wait_ge(s_prTc, 2 * g + t + 1)
                        pe.wait_ge(s_attn, 2 * g + t + CREDIT)
                        for j in range(T):
                            mm = pe.matmul(p_small[:, 16 * t:16 * t + DH + 1], probsT[:, t, j * P:(j + 1) * P],
                                           v_ext[:, j, bass.ds(h, 1), :], start=(j == 0), stop=(j == T - 1))
                        mm.then_inc(s_av, 1)
                pe.wait_ge(s_attn, 2 * H * (n + 1) + CREDIT)
                for t in range(T):
                    mm = pe.transpose(p_tr[:, t * P:(t + 1) * P], attn[:, t, :], ident[:, :])
                mm.then_inc(s_aT, 1)
                for t in range(T):
                    pe.matmul(p_proj[1][:, t * P:(t + 1) * P], xnT[:, t * P:(t + 1) * P], w_ffn[:, :], start=True, stop=True)
                pe.wait_ge(s_aTc, n + 1)
                for t in range(T):
                    mm = pe.matmul(p_proj[0][:, t * P:(t + 1) * P], attnT[:, t * P:(t + 1) * P], w_o[:, :], start=True, stop=True)
                mm.then_inc(s_y, 1)

        @block.scalar
        def _(act):
            act.sem_inc(s_exp, CREDIT)
            act.wait_ge(s_wfT, 1)
            act.activation(w_ffn_sign[:, :], p_tr[:, 0:P], ACT.Sign).then_inc(s_wsign, 1)
            with act.Fori(0, B) as n:
                act.wait_ge(s_xT, n + 1)
                act.copy(xnT[:, :], p_tr[:, 0:S]).then_inc(s_xnT, 1)
                act.wait_ge(s_qkvg, 2 * n + 2)
                act.activation(gate_e[:, :, :], qkvg[:, :, 3 * D:4 * D], ACT.Exp, scale=-1.0).then_inc(s_gexp, 1)
                act.copy(v_ext[:, :, :, 0:DH], qkvg[:, :, 2 * D:3 * D].rearrange("p t (h d) -> p t h d", h=H)).then_inc(s_vext, 1)
                act.wait_ge(s_tz, n + 1)
                act.activation(temp_w[:, 1:2], temp_w[:, 0:1], ACT.Exp, scale=-1.0).then_inc(s_texp, 1)
                act.wait_ge(s_qkT, n + 1)
                act.mul(rest[:, 0:S], p_tr[:, 0:S], Q_SCALE).then_inc(s_rest, 1)
                act.copy(rest[:, S:2 * S], p_tr[:, S:2 * S]).then_inc(s_rest, 1)
                act.wait_ge(s_escale, n + 1)
                with act.Fori(0, H) as h:
                    g = n * H + h
                    for t in range(T):
                        act.wait_ge(s_copied, g + 1)
                        act.wait_ge(s_probs, 2 * g + t + CREDIT)
                        act.activation(expd[:, t, :], p_score[t][:, 0:S], ACT.Exp, scale=exp_scale[:, 0:1]).then_inc(s_exp, 1)
                    for t in range(T):
                        act.wait_ge(s_prT, 2 * g + t + 1 + CREDIT)
                        act.copy(probsT[:, t, :], p_prT[t][:, 0:S]).then_inc(s_prTc, 1)
                act.wait_ge(s_aT, n + 1)
                act.copy(attnT[:, :], p_tr[:, 0:S]).then_inc(s_aTc, 1)

        @block.vector
        def _(dve):
            for handed_back in (s_res, s_probs, s_attn):
                dve.sem_inc(handed_back, CREDIT)
            dve.wait_ge(s_const, 16 * N_CONST)
            dve.wait_ge(s_wsign, 1)
            dve.wait_ge(s_ident, 4)
            dve.tensor_tensor(w_ffn[:, :], w_ffn_sign[:, :], ident[:, :], ALU.add).then_inc(s_setup, 1)
            dve.tensor_copy(wt_wide[:, :], wt_col[:, 0:1].broadcast_to([P, P])).then_inc(s_setup, 1)
            with dve.Fori(0, B) as n:
                link = chain(dve, s_fchain)
                dve.wait_ge(s_x, 16 * n + 16)
                for t in range(T):
                    link(dve.bn_stats(bn[:, t, :], x_in[:, t, :]))
                for t in range(T):
                    link(dve.bn_aggr(mv[:, t, :], bn[:, t, :]))
                dve.tensor_scalar(var_eps[:, :], mv[:, :, 1], EPS_LN, None, ALU.add).then_inc(s_var, 1)
                dve.wait_ge(s_rstd0, n + 1)
                dve.wait_ge(s_var, n + 1)
                link(dve.tensor_tensor(rstd_t[:, :], rstd0[:, :], rstd0[:, :], ALU.mult))
                link(dve.tensor_tensor(rstd_t[:, :], rstd_t[:, :], var_eps[:, :], ALU.mult))
                link(dve.tensor_scalar(rstd_t[:, :], rstd_t[:, :], -0.5, 1.5, ALU.mult, ALU.add))
                link(dve.tensor_tensor(rstd[:, :], rstd_t[:, :], rstd0[:, :], ALU.mult))
                for t in range(T):
                    ins = dve.tensor_scalar(xn[:, t, :], x_in[:, t, :], mv[:, t, 0:1], rstd[:, t:t + 1], ALU.subtract, ALU.mult)
                    if t == 0:
                        link(ins)
                ins.then_inc(s_xn, 1)
                dve.wait_ge(s_xnT, n + 1)
                dve.tensor_reduce(xsum[:, :], xnT[:, :], AX.X, ALU.add).then_inc(s_xsum, 1)
                for t in range(T):
                    dve.wait_ge(s_proj, 2 * n + t + 1)
                    dve.tensor_tensor(qkvg[:, t, :], p_proj[t][:, :], bias_all[:, :], ALU.add).then_inc(s_qkvg, 1)
                dve.wait_ge(s_z, n + 1)
                dve.tensor_scalar(temp_w[:, 0:1], p_small[:, 32:33], 1.0 / S, bias_t[:, 0:1], ALU.mult, ALU.add).then_inc(s_tz, 1)
                dve.wait_ge(s_sq, n + 1)
                link(dve.tensor_reduce(norm2[:, :], sq[:, :, :].rearrange("p t (c d) -> p (t c) d", d=DH), AX.X, ALU.add))
                dve.tensor_scalar(norm2[:, :], norm2[:, :], NORM_FLOOR ** 2, None, ALU.max).then_inc(s_norm2, 1)
                dve.wait_ge(s_texp, n + 1)
                link(dve.tensor_scalar(temp_w[:, 2:3], temp_w[:, 1:2], 1.0, None, ALU.add))
                link(dve.reciprocal(temp_w[:, 3:4], temp_w[:, 2:3]))
                link(dve.tensor_scalar(temp_w[:, 4:5], temp_w[:, 3:4], 0.5, Q_SCALE, ALU.add, ALU.mult))
                dve.reciprocal(exp_scale[:, :], temp_w[:, 4:5]).then_inc(s_escale, 1)
                dve.wait_ge(s_inv0, n + 1)
                dve.wait_ge(s_norm2, n + 1)
                link(dve.tensor_tensor(inv_t[:, :], inv0[:, :], inv0[:, :], ALU.mult))
                link(dve.tensor_tensor(inv_t[:, :], inv_t[:, :], norm2[:, :], ALU.mult))
                link(dve.tensor_scalar(inv_t[:, :], inv_t[:, :], -0.5, 1.5, ALU.mult, ALU.add))
                link(dve.tensor_tensor(inv[:, :], inv_t[:, :], inv0[:, :], ALU.mult))
                dve.wait_ge(s_qkvg, 2 * n + 2)
                for t in range(T):
                    dve.tensor_tensor(qkn[:, t, :].rearrange("p (c d h) -> p c h d", c=2, d=DH),
                                      qkvg[:, t, 0:2 * D].rearrange("p (c h d) -> p c h d", c=2, d=DH),
                                      inv[:, t * 2 * H:(t + 1) * 2 * H].rearrange("p (c h a) -> p c h a", c=2, a=1).broadcast_to([P, 2, H, DH]),
                                      ALU.mult).then_inc(s_qkn, 1)
                dve.wait_ge(s_gexp, n + 1)
                link(dve.tensor_scalar(gate_e[:, :, :], gate_e[:, :, :], 1.0, None, ALU.add))
                link(dve.reciprocal(gate[:, :, :], gate_e[:, :, :]))
                with dve.Fori(0, H) as h:
                    g = n * H + h
                    hlink = chain(dve, s_hchain)
                    for t in range(T):
                        dve.sem_clear(s_round[t])
                    for t in range(T):
                        dve.wait_ge(s_score, 2 * g + t + 1)
                        dve.tensor_copy(work[:, t, :], p_score[t][:, 0:S]).then_inc(s_round[t], 1)
                    dve.memset(copied_mark[:, :], 0.0).then_inc(s_copied, 1)
                    for r in range(KEEP // 8):
                        for t in range(T):
                            dve.wait_ge(s_round[t], 2 * r + 1)
                            dve.max(top8[:, t, :], work[:, t, :]).then_inc(s_round[t], 1)
                        for t in range(T):
                            dve.wait_ge(s_round[t], 2 * r + 2)
                            dve.match_replace(work[:, t, :], top8[:, t, :], work[:, t, :], REMOVED).then_inc(s_round[t], 1)
                    for t in range(T):
                        dve.wait_ge(s_round[t], KEEP // 4 + 1)
                        dve.wait_ge(s_exp, 2 * g + t + 1 + CREDIT)
                        dve.wait_ge(s_prT, 2 * g + t + CREDIT)
                        dve.scalar_tensor_tensor(out=probs[:, t, :], in0=work[:, t, :], scalar=IS_REMOVED, in1=expd[:, t, :],
                                                 op0=ALU.is_lt, op1=ALU.mult).then_inc(s_probs, 1)
                    for t in range(T):
                        dve.wait_ge(s_av, 2 * g + t + 1)
                        o = p_small[:, 16 * t:16 * t + DH + 1]
                        hlink(dve.reciprocal(rden[:, t:t + 1], o[:, DH:DH + 1]))
                        dve.tensor_scalar(attn[:, t, bass.ds(h * DH, DH)], o[:, 0:DH], rden[:, t:t + 1], None,
                                          ALU.mult).then_inc(s_attn, 1)
                blink = chain(dve, s_bchain)
                dve.wait_ge(s_y, n + 1)
                link3 = p_proj[0][:, 0:S].rearrange("p (t d) -> p t d", t=T)
                blink(dve.tensor_tensor(mix[:, :, :], link3, xn[:, :, :], ALU.subtract))
                blink(dve.tensor_tensor(mix[:, :, :], mix[:, :, :], bias_o[:, :, :], ALU.add))
                blink(dve.tensor_tensor(mix[:, :, :], mix[:, :, :], gate[:, :, :], ALU.mult))
                blink(dve.tensor_tensor(base[:, :, :], p_proj[1][:, 0:S].rearrange("p (t d) -> p t d", t=T), x_in[:, :, :], ALU.add))
                dve.wait_ge(s_out, 16 * n + DMA_CREDIT)
                dve.tensor_tensor(res[:, :, :], base[:, :, :], mix[:, :, :], ALU.add).then_inc(s_res, 1)


_INS = ["L0_attn_x", "L0_attn_Wq", "L0_attn_bq", "L0_attn_Wk", "L0_attn_bk", "L0_attn_Wv", "L0_attn_bv", "L0_attn_Wo",
        "L0_attn_bo", "L0_attn_Wt", "L0_attn_bt", "L0_attn_Wg", "L0_attn_bg", "L0_ffn_weight"]


def kernel(**inputs):
    import numpy as _np
    import concourse.bacc as _bacc
    from concourse import mybir as _mybir
    from concourse.bass_utils import run_bass_kernel_spmd as _run

    nc = _bacc.Bacc("TRN2", target_bir_lowering=False, num_devices=1)
    arrays, args = {}, []
    for name in _INS:
        a = _np.ascontiguousarray(inputs[name])
        arrays[f"in_{name}"] = a
        args.append(nc.dram_tensor(f"in_{name}", a.shape, _mybir.dt.from_np(a.dtype), kind="ExternalInput").ap())
    args.append(nc.dram_tensor("out_0", (B, S, D), _mybir.dt.float32, kind="ExternalOutput").ap())
    build(nc, *args)
    r = _run(nc, [arrays], core_ids=[0])
    return r.results[0]["out_0"]
```
